# Optimizing a Trainium2 kernel written in Bass

```python
import numpy as np
import jax
import jax.numpy as jnp

def _softmax(x, axis=-1):
    return jax.nn.softmax(x, axis=axis)

def _gelu(x):
    return jax.nn.gelu(x, approximate=True)

def _silu(x):
    return jax.nn.silu(x)

def _sigmoid(x):
    return jax.nn.sigmoid(x)

def _layernorm(x, axis=-1, eps=1e-05):
    m = jnp.mean(x, axis=axis, keepdims=True)
    v = jnp.var(x, axis=axis, keepdims=True)
    return (x - m) / jnp.sqrt(v + eps)

def _scatter_add(tgt, idx, src, axis=0):
    return tgt.at[idx].add(src)

def _segment_sum(src, seg, n):
    return jax.ops.segment_sum(src, seg, n)
kernel_name = 'mk_dlrm_tower_d1_rec_r8_7f6306'

def setup_inputs(seed: int=0):
    np.random.seed(seed)
    _w = jnp.asarray

    def _rec_inputs():
        import jax
        import jax.numpy as jnp
        _tk = jax.random.key(seed)
        ids = jnp.stack([jax.random.randint(jax.random.fold_in(_tk, 200 + f), (512,), 0, v, jnp.int32) for f, v in enumerate([125000, 1000, 12500, 12500, 12500, 1250, 1000, 12500, 12500, 1250, 12500, 12500, 1250, 12500, 1000, 1250, 1250, 1250, 1000, 1000, 1000, 1000, 1000, 1250, 1250, 1250])], axis=1)
        tbl_0 = 0.05 * jax.random.normal(jax.random.fold_in(_tk, 500 + 0), (125000, 128), jnp.float32)
        tbl_1 = 0.05 * jax.random.normal(jax.random.fold_in(_tk, 500 + 1), (1000, 128), jnp.float32)
        tbl_2 = 0.05 * jax.random.normal(jax.random.fold_in(_tk, 500 + 2), (12500, 128), jnp.float32)
        tbl_3 = 0.05 * jax.random.normal(jax.random.fold_in(_tk, 500 + 3), (12500, 128), jnp.float32)
        tbl_4 = 0.05 * jax.random.normal(jax.random.fold_in(_tk, 500 + 4), (12500, 128), jnp.float32)
        tbl_5 = 0.05 * jax.random.normal(jax.random.fold_in(_tk, 500 + 5), (1250, 128), jnp.float32)
        tbl_6 = 0.05 * jax.random.normal(jax.random.fold_in(_tk, 500 + 6), (1000, 128), jnp.float32)
        tbl_7 = 0.05 * jax.random.normal(jax.random.fold_in(_tk, 500 + 7), (12500, 128), jnp.float32)
        tbl_8 = 0.05 * jax.random.normal(jax.random.fold_in(_tk, 500 + 8), (12500, 128), jnp.float32)
        tbl_9 = 0.05 * jax.random.normal(jax.random.fold_in(_tk, 500 + 9), (1250, 128), jnp.float32)
        tbl_10 = 0.05 * jax.random.normal(jax.random.fold_in(_tk, 500 + 10), (12500, 128), jnp.float32)
        tbl_11 = 0.05 * jax.random.normal(jax.random.fold_in(_tk, 500 + 11), (12500, 128), jnp.float32)
        tbl_12 = 0.05 * jax.random.normal(jax.random.fold_in(_tk, 500 + 12), (1250, 128), jnp.float32)
        tbl_13 = 0.05 * jax.random.normal(jax.random.fold_in(_tk, 500 + 13), (12500, 128), jnp.float32)
        tbl_14 = 0.05 * jax.random.normal(jax.random.fold_in(_tk, 500 + 14), (1000, 128), jnp.float32)
        tbl_15 = 0.05 * jax.random.normal(jax.random.fold_in(_tk, 500 + 15), (1250, 128), jnp.float32)
        tbl_16 = 0.05 * jax.random.normal(jax.random.fold_in(_tk, 500 + 16), (1250, 128), jnp.float32)
        tbl_17 = 0.05 * jax.random.normal(jax.random.fold_in(_tk, 500 + 17), (1250, 128), jnp.float32)
        tbl_18 = 0.05 * jax.random.normal(jax.random.fold_in(_tk, 500 + 18), (1000, 128), jnp.float32)
        tbl_19 = 0.05 * jax.random.normal(jax.random.fold_in(_tk, 500 + 19), (1000, 128), jnp.float32)
        tbl_20 = 0.05 * jax.random.normal(jax.random.fold_in(_tk, 500 + 20), (1000, 128), jnp.float32)
        tbl_21 = 0.05 * jax.random.normal(jax.random.fold_in(_tk, 500 + 21), (1000, 128), jnp.float32)
        tbl_22 = 0.05 * jax.random.normal(jax.random.fold_in(_tk, 500 + 22), (1000, 128), jnp.float32)
        tbl_23 = 0.05 * jax.random.normal(jax.random.fold_in(_tk, 500 + 23), (1250, 128), jnp.float32)
        tbl_24 = 0.05 * jax.random.normal(jax.random.fold_in(_tk, 500 + 24), (1250, 128), jnp.float32)
        tbl_25 = 0.05 * jax.random.normal(jax.random.fold_in(_tk, 500 + 25), (1250, 128), jnp.float32)
        _rk = jax.random.fold_in(_tk, 7)
        r_dense_features = -0.000520686 + 1.00062 * jax.random.normal(jax.random.fold_in(_rk, 101), (512, 128), jnp.float32)
        W_top1 = 0.0405887 * jax.random.normal(jax.random.fold_in(_tk, 801), (607, 512), jnp.float32)
        W_top2 = 0.0441942 * jax.random.normal(jax.random.fold_in(_tk, 802), (512, 256), jnp.float32)
        W_top3 = 0.0625 * jax.random.normal(jax.random.fold_in(_tk, 803), (256, 1), jnp.float32)
        b_top1 = jnp.zeros((512,), jnp.float32)
        b_top2 = jnp.zeros((256,), jnp.float32)
        return (r_dense_features, ids, tbl_0, tbl_1, tbl_2, tbl_3, tbl_4, tbl_5, tbl_6, tbl_7, tbl_8, tbl_9, tbl_10, tbl_11, tbl_12, tbl_13, tbl_14, tbl_15, tbl_16, tbl_17, tbl_18, tbl_19, tbl_20, tbl_21, tbl_22, tbl_23, tbl_24, tbl_25, W_top1, b_top1, W_top2, b_top2, W_top3)
    r_dense_features, ids, tbl_0, tbl_1, tbl_2, tbl_3, tbl_4, tbl_5, tbl_6, tbl_7, tbl_8, tbl_9, tbl_10, tbl_11, tbl_12, tbl_13, tbl_14, tbl_15, tbl_16, tbl_17, tbl_18, tbl_19, tbl_20, tbl_21, tbl_22, tbl_23, tbl_24, tbl_25, W_top1, b_top1, W_top2, b_top2, W_top3 = _rec_inputs()

    def _L0_rec_setup():
        import jax, jax.numpy as jnp
        import numpy as np
        F = 26
        N = F + 1
        _TRIU_I, _TRIU_J = np.triu_indices(N, k=1)
        key = jax.random.key(seed)
        k1, k2 = jax.random.split(key)
        B, D = (2048, 128)
        dense_features = jax.random.normal(k1, (B, D), dtype=jnp.float32)
        sparse_features = jax.random.normal(k2, (B, F, D), dtype=jnp.float32)
        return {'dense_features': dense_features, 'sparse_features': sparse_features}
    _L0_rec_all = _L0_rec_setup()
    _L0_rec_in = {k: v for k, v in _L0_rec_all.items() if k in ()}
    del _L0_rec_all
    return {'r_dense_features': r_dense_features, 'ids': ids, 'tbl_0': tbl_0, 'tbl_1': tbl_1, 'tbl_2': tbl_2, 'tbl_3': tbl_3, 'tbl_4': tbl_4, 'tbl_5': tbl_5, 'tbl_6': tbl_6, 'tbl_7': tbl_7, 'tbl_8': tbl_8, 'tbl_9': tbl_9, 'tbl_10': tbl_10, 'tbl_11': tbl_11, 'tbl_12': tbl_12, 'tbl_13': tbl_13, 'tbl_14': tbl_14, 'tbl_15': tbl_15, 'tbl_16': tbl_16, 'tbl_17': tbl_17, 'tbl_18': tbl_18, 'tbl_19': tbl_19, 'tbl_20': tbl_20, 'tbl_21': tbl_21, 'tbl_22': tbl_22, 'tbl_23': tbl_23, 'tbl_24': tbl_24, 'tbl_25': tbl_25, 'W_top1': W_top1, 'b_top1': b_top1, 'W_top2': W_top2, 'b_top2': b_top2, 'W_top3': W_top3}

def reference(r_dense_features, ids, tbl_0, tbl_1, tbl_2, tbl_3, tbl_4, tbl_5, tbl_6, tbl_7, tbl_8, tbl_9, tbl_10, tbl_11, tbl_12, tbl_13, tbl_14, tbl_15, tbl_16, tbl_17, tbl_18, tbl_19, tbl_20, tbl_21, tbl_22, tbl_23, tbl_24, tbl_25, W_top1, b_top1, W_top2, b_top2, W_top3):
    import jax
    import jax.numpy as jnp

    def _L0_rec_ref(dense_features, sparse_features):
        import jax, jax.numpy as jnp
        import numpy as np
        F = 26
        N = F + 1
        _TRIU_I, _TRIU_J = np.triu_indices(N, k=1)
        combined = jnp.concatenate([dense_features[:, None, :], sparse_features], axis=1)
        interactions = jnp.einsum('bnd,bmd->bnm', combined, combined)
        interactions_flat = interactions[:, _TRIU_I, _TRIU_J]
        return jnp.concatenate([dense_features, interactions_flat], axis=1)
    e = jnp.stack([tbl_0[ids[:, 0]], tbl_1[ids[:, 1]], tbl_2[ids[:, 2]], tbl_3[ids[:, 3]], tbl_4[ids[:, 4]], tbl_5[ids[:, 5]], tbl_6[ids[:, 6]], tbl_7[ids[:, 7]], tbl_8[ids[:, 8]], tbl_9[ids[:, 9]], tbl_10[ids[:, 10]], tbl_11[ids[:, 11]], tbl_12[ids[:, 12]], tbl_13[ids[:, 13]], tbl_14[ids[:, 14]], tbl_15[ids[:, 15]], tbl_16[ids[:, 16]], tbl_17[ids[:, 17]], tbl_18[ids[:, 18]], tbl_19[ids[:, 19]], tbl_20[ids[:, 20]], tbl_21[ids[:, 21]], tbl_22[ids[:, 22]], tbl_23[ids[:, 23]], tbl_24[ids[:, 24]], tbl_25[ids[:, 25]]], axis=1)
    z = _L0_rec_ref(r_dense_features, e)
    z = z.reshape(z.shape[0], -1)
    h = jnp.concatenate([z, r_dense_features], axis=1)
    h = jnp.maximum(h @ W_top1 + b_top1, 0.0)
    h = jnp.maximum(h @ W_top2 + b_top2, 0.0)
    y = h @ W_top3
    return y

_drawn_inputs = setup_inputs


def setup_inputs(seed=0):
    import zlib

    import numpy as np

    out = dict(_drawn_inputs(seed))
    spreads = {'b_top1': (0.0, 0.1), 'b_top2': (0.0, 0.1)}
    factors = {}
    for name, (base, spread) in spreads.items():
        noise = np.random.default_rng([zlib.crc32(name.encode()), seed]).standard_normal(out[name].shape)
        drawn = base * np.exp(spread * noise) if base else spread * noise
        out[name] = jnp.asarray(drawn.astype(out[name].dtype))
    for name, factor in factors.items():
        out[name] = (out[name] * factor).astype(out[name].dtype)
    return out
```

```python
from contextlib import ExitStack

import concourse.bass as bass
from concourse import mybir

F32 = mybir.dt.float32
I32 = mybir.dt.int32
U32 = mybir.dt.uint32
F32R = mybir.dt.float32r
ALU = mybir.AluOpType
ACT = mybir.ActivationFunctionType

P = 128
B = 512
D = 128
F = 26
N = F + 1
TILES = B // P
H1, H2 = 512, 256
QUAD = 32
QUADS = P // QUAD
BLOCKS = P // QUADS
CHUNKS = 6
REPEAT = 2
ROWS = N + REPEAT
TABLE_ROWS = [125000, 1000, 12500, 12500, 12500, 1250, 1000, 12500, 12500, 1250, 12500, 12500, 1250,
              12500, 1000, 1250, 1250, 1250, 1000, 1000, 1000, 1000, 1000, 1250, 1250, 1250]
LOOKED_UP = 7
by_size = sorted(range(F), key=lambda f: TABLE_ROWS[f])
LOOKUPS = by_size[:LOOKED_UP]
GATHERED = by_size[LOOKED_UP:]
SLOT_TABLE = [None] + GATHERED + LOOKUPS
TURNED = 1 + len(GATHERED)
FULL = [TABLE_ROWS[f] // P for f in LOOKUPS]
LAST = [TABLE_ROWS[f] % P for f in LOOKUPS]
MAX_BLOCKS = max(FULL) + 1
BY_SCALAR = 2
SIZES = sorted(set(FULL))
PER_GROUP = 4
GROUPS = [list(range(a, min(a + PER_GROUP, TURNED))) for a in range(0, TURNED, PER_GROUP)]
NG = len(GROUPS)
QUARTERS = H1 // P
FIRST_TURNS = [("turn", t, g) for t in range(2) for g in range(NG)]
FIRST_LOOKS = [("look", j, 0) for j in range(LOOKED_UP)]
FIRST_STEPS = [x for pair in zip(FIRST_TURNS, FIRST_LOOKS) for x in pair] + FIRST_TURNS[LOOKED_UP:]


def first_layer(t):
    return [("layer1", t, q) for q in range(QUARTERS)]


def alternate(t, earlier, between):
    turns, quarters = [("turn", t, g) for g in range(NG)], first_layer(earlier)
    steps = turns[:2] + between
    for n in range(QUARTERS):
        steps += [quarters[n]] + turns[2 + n:3 + n]
    return steps


TENSOR_STEPS = (
    FIRST_STEPS + [("products", 0, 0), ("products", 1, 0)]
    + alternate(2, 1, first_layer(0) + [("layer2", 0, 0)]) + [("layer3", 0, 0), ("products", 2, 0)]
    + alternate(3, 2, [("layer2", 1, 0)]) + [("layer3", 1, 0), ("products", 3, 0), ("layer2", 2, 0)]
    + first_layer(3) + [("layer3", 2, 0), ("layer2", 3, 0), ("layer3", 3, 0)]
)
UNITS = [x for x in TENSOR_STEPS if x[0] in ("turn", "look")]
VECTOR_STEPS = [
    ("products", 0), ("products", 1), ("turn", 2), ("layer3", 0), ("products", 2),
    ("turn", 3), ("layer3", 1), ("products", 3), ("layer3", 2), ("layer3", 3),
]
SCALAR_STEPS = [
    ("extra", 1), ("products", 0), ("products", 1), ("extra", 2), ("layer1", 0), ("layer2", 0),
    ("layer1", 1), ("products", 2), ("extra", 3), ("layer2", 1), ("layer1", 2),
    ("products", 3), ("layer2", 2), ("layer1", 3), ("layer2", 3),
]
FIRST_SLOT = [6, 12, 18, 0]
LATE_SLOT = 24


def product_rows():
    where = {}
    for q in range(QUADS):
        for c in range(CHUNKS):
            late = q == QUADS - 1 and c < N - LATE_SLOT
            m = LATE_SLOT + c if late else FIRST_SLOT[q] + c
            for n in range(m):
                where[c, QUAD * q + n] = (n, m)
            if late:
                for n in range(c):
                    where[c, QUAD * q + N + n] = (n, c)
    assert sorted(where.values()) == [(n, m) for n in range(N) for m in range(n + 1, N)]
    return where


def dlrm_tower(nc, dense, ids, ids_t, tables, w1, w2, small, out):
    with ExitStack() as ctx:
        def sb(name, shape, dt=F32):
            return ctx.enter_context(nc.sbuf_tensor(name, shape, dt))

        def psum(name, shape):
            return ctx.enter_context(nc.psum_tensor(name, shape, F32))

        def sem(name):
            return ctx.enter_context(nc.semaphore(name))

        idx = sb("idx", [P, TILES, F], I32)
        dense_rows = sb("dense_rows", [P, TILES, D])
        vecs = sb("vecs", [P, 2, TURNED, D])
        vecs_t = sb("vecs_t", [P, TILES, P, ROWS])
        dense_t = sb("dense_t", [P, TILES, P])
        ident = sb("ident", [P, P])
        w1_sb = sb("w1_sb", [P, 2 + CHUNKS, H1])
        w_dense = sb("w_dense", [P, H1])
        w2_sb = sb("w2_sb", [P, H1 // P, H2])
        small_sb = sb("small_sb", [P, 8])
        b1_col, b2_col, w3_col = small_sb[:, 0:4], small_sb[:, 4:6], small_sb[:, 6:8]
        prods = sb("prods", [P, TILES, CHUNKS, P])
        h1 = sb("h1", [P, 2, H1 // P, P])
        h2 = sb("h2", [P, 2, H2 // P, P])
        y_sb = sb("y_sb", [1, B])
        ids_all = sb("ids_all", [P, LOOKED_UP, B], I32)
        row_of = sb("row_of", [P, len(SIZES), MAX_BLOCKS])
        table = sb("table", [P, 2, MAX_BLOCKS, D])
        table_hi = sb("table_hi", [P, 2, MAX_BLOCKS, D], F32R)
        table_lo = sb("table_lo", [P, 2, MAX_BLOCKS, D], F32R)
        one_hot = sb("one_hot", [P, 2, MAX_BLOCKS, B], F32R)

        turned = [psum(f"turned{i}", [P, PER_GROUP, P]) for i in range(2)]
        gram = [psum(f"gram{i}", [P, BLOCKS, QUAD]) for i in range(2)]
        h1_ps = psum("h1_ps", [P, H1 // P, P])
        h2_ps = psum("h2_ps", [P, H1 // P, P])

        idx_in = sem("idx_in")
        dense_in = sem("dense_in")
        w_in = sem("w_in")
        distance = sb("distance", [P, BY_SCALAR, B])
        one = sb("one", [P, 1])
        one_ok = sem("one_ok")
        distance_ok = sem("distance_ok")
        hot_scalar = sem("hot_scalar")
        ids_all_in = [sem(f"ids_all_in{j}") for j in range(LOOKED_UP)]
        table_in = [sem(f"table_in{i}") for i in range(2)]
        table_zero = sem("table_zero")
        rows_ok = sem("rows_ok")
        hi_ok = sem("hi_ok")
        lo_ok = sem("lo_ok")
        hot_ok = sem("hot_ok")
        look_ok = sem("look_ok")
        look_out = sem("look_out")
        gathered = [[sem(f"gathered{t}_{g}") for g in range(len(GROUPS))] for t in range(TILES)]
        ident_zero = sem("ident_zero")
        ident_ok = sem("ident_ok")
        prods_zero = sem("prods_zero")
        w_dense_ok = sem("w_dense_ok")
        turned_ok = sem("turned_ok")
        slots_out = sem("slots_out")
        extra_out = sem("extra_out")
        gram_ok = sem("gram_ok")
        prods_dve = sem("prods_dve")
        prods_act = sem("prods_act")
        h1_ok = sem("h1_ok")
        h1_out = sem("h1_out")
        h2_ok = sem("h2_ok")
        h2_out = sem("h2_out")
        y_ok = sem("y_ok")
        y_out = sem("y_out")
        stored = sem("stored")

        BY_ENGINE = 2 * (QUADS + 1)

        def copy_products(engine, copy, done, t, quads):
            engine.wait_ge(gram_ok, t + 1)
            for i, q in enumerate(quads):
                src = gram[t % 2][QUAD * q:QUAD * (q + 1), :, :]
                for k in [3, 0, 1, 2]:
                    copy(prods[QUAD * k:QUAD * k + ROWS, t, :, q::QUADS],
                         src[0:ROWS, :, FIRST_SLOT[k]:FIRST_SLOT[k] + CHUNKS]
                         .rearrange("p b c -> p c b")).then_inc(done, 1)
                engine.wait_ge(done, BY_ENGINE * t + (QUADS + 1) * i + 1)
                copy(prods[QUAD * 3:QUAD * 3 + N, t, 0:N - LATE_SLOT, q::QUADS],
                     src[0:N, :, LATE_SLOT:N].rearrange("p b c -> p c b")).then_inc(done, 1)

        block = ctx.enter_context(nc.Block())

        @block.sync
        def _(sp):
            sp.dma_start(idx[:], ids.rearrange("(t p) f -> p t f", p=P)).then_inc(idx_in, 16)

            def load_table(j):
                f, full, last = LOOKUPS[j], FULL[j], LAST[j]
                if j == 0:
                    sp.wait_ge(table_zero, 1)
                if j >= 2:
                    sp.wait_ge(lo_ok, j - 1)
                sp.dma_start(table[:, j % 2, 0:full, :],
                             tables[f][0:full * P, :].rearrange("(p c) d -> p c d", p=P))\
                    .then_inc(table_in[j % 2], 16)
                sp.dma_start(table[0:last, j % 2, full, :], tables[f][full * P:full * P + last, :])\
                    .then_inc(table_in[j % 2], 16)
                sp.dma_start(ids_all[:, j, :], ids_t[f:f + 1, :].to_broadcast([P, B]))\
                    .then_inc(ids_all_in[j], 16)

            load_table(0)
            sp.dma_start(dense_rows[:], dense.rearrange("(t p) d -> p t d", p=P)).then_inc(dense_in, 16)
            for j in range(1, LOOKED_UP):
                load_table(j)
            sp.dma_start(w1_sb[:], w1).then_inc(w_in, 16)
            sp.dma_start(w2_sb[:], w2).then_inc(w_in, 16)
            sp.dma_start(small_sb[:], small).then_inc(w_in, 16)
            sp.wait_ge(y_out, TILES)
            sp.dma_start(out.rearrange("b o -> o b"), y_sb[:]).then_inc(stored, 16)
            sp.wait_ge(stored, 16)

        @block.gpsimd
        def _(pool):
            nc.gpsimd.memset(ident[:], 0.0).then_inc(ident_zero, 1)
            pool.wait_ge(ident_zero, 1)
            nc.gpsimd.affine_select(out=ident[:], in_=ident[:], compare_op=ALU.not_equal, fill=1.0, base=0,
                                    pattern=[[-1, P]], channel_multiplier=1).then_inc(ident_ok, 1)
            nc.gpsimd.memset(table[:], 0.0).then_inc(table_zero, 1)
            for i, full in enumerate(SIZES):
                nc.gpsimd.iota(row_of[:, i, 0:full], pattern=[[1, full]], base=0, channel_multiplier=full,
                               allow_small_or_imprecise_dtypes=True).then_inc(rows_ok, 1)
                nc.gpsimd.iota(row_of[:, i, full:full + 1], pattern=[[1, 1]], base=full * P,
                               channel_multiplier=1,
                               allow_small_or_imprecise_dtypes=True).then_inc(rows_ok, 1)
            pool.wait_ge(idx_in, 16)
            for t in range(TILES):
                for g, slots in enumerate(GROUPS):
                    if t >= 2:
                        pool.wait_ge(turned_ok, NG * (t - 2) + g + 1)
                    for s in slots:
                        if s:
                            f = SLOT_TABLE[s]
                            nc.gpsimd.indirect_dma_start(
                                out=vecs[:, t % 2, s, :], out_offset=None, in_=tables[f],
                                in_offset=bass.IndirectOffsetOnAxis(
                                    ap=idx[:, t, f:f + 1].bitcast(U32), axis=0),
                            ).then_inc(gathered[t][g], 16)

        @block.tensor
        def _(pe):
            def mlp1(t, o):
                if o == 0:
                    first_layer_ready(t)
                cols = slice(o * P, (o + 1) * P)
                nc.tensor.matmul(h1_ps[:, o, :], w_dense[:, cols], dense_t[:, t, :], start=True, stop=False)
                for c in range(CHUNKS):
                    mm = nc.tensor.matmul(h1_ps[:, o, :], w1_sb[:, 2 + c, cols], prods[:, t, c, :],
                                          start=False, stop=(c == CHUNKS - 1))
                if o == QUARTERS - 1:
                    mm.then_inc(h1_ok, 1)

            def first_layer_ready(t):
                pe.wait_ge(prods_dve, BY_ENGINE * (t + 1))
                pe.wait_ge(prods_act, BY_ENGINE * (t + 1))
                if t == 0:
                    pe.wait_ge(w_in, 48)
                    pe.wait_ge(w_dense_ok, 1)
                if t >= 1:
                    pe.wait_ge(h1_out, 4 * t)

            def mlp2(t):
                pe.wait_ge(h1_out, 4 * (t + 1))
                if t >= 1:
                    pe.wait_ge(y_out, t)
                for o in range(H2 // P):
                    for c in range(H1 // P):
                        mm = nc.tensor.matmul(h2_ps[:, o, :], w2_sb[:, c, o * P:(o + 1) * P], h1[:, t % 2, c, :],
                                              start=(c == 0), stop=(c == H1 // P - 1))
                mm.then_inc(h2_ok, 1)

            def mlp3(t):
                pe.wait_ge(h2_out, 2 * (t + 1))
                for c in range(H2 // P):
                    mm = nc.tensor.matmul(h2_ps[0:1, 3, :], w3_col[:, c:c + 1], h2[:, t % 2, c, :],
                                          start=(c == 0), stop=(c == H2 // P - 1))
                mm.then_inc(y_ok, 1)

            def bank_free(k):
                if k < 2:
                    return
                before = UNITS[:k - 1]
                if before[-1][0] == "look":
                    pe.wait_ge(look_out, sum(u[0] == "look" for u in before))
                else:
                    pe.wait_ge(slots_out, sum(u[0] == "turn" for u in before))

            def turn(k, t, g):
                slots = GROUPS[g]
                pe.wait_ge(gathered[t][g], 16 * sum(s > 0 for s in slots))
                bank_free(k)
                for j, s in enumerate(slots):
                    mm = nc.tensor.transpose(turned[k % 2][:, j, :],
                                             vecs[:, t % 2, s, :] if s else dense_rows[:, t, :], ident[:])
                mm.then_inc(turned_ok, 1)

            def look_up(k, j):
                bank_free(k)
                pe.wait_ge(lo_ok, j + 1)
                for c in range(FULL[j] + 1):
                    rows = P if c < FULL[j] else LAST[j]
                    by_vector = FULL[j] + 1 - BY_SCALAR
                    if c < by_vector:
                        pe.wait_ge(hot_ok, sum(n + 1 - BY_SCALAR for n in FULL[:j]) + c + 1)
                    else:
                        pe.wait_ge(hot_scalar, BY_SCALAR * j + c - by_vector + 1)
                    for part in (table_hi, table_lo):
                        mm = nc.tensor.matmul(turned[k % 2].rearrange("p s r -> p (s r)"),
                                              part[0:rows, j % 2, c, :], one_hot[0:rows, j % 2, c, :],
                                              start=(c == 0 and part is table_hi),
                                              stop=(c == FULL[j] and part is table_lo))
                mm.then_inc(look_ok, 1)

            def products(t):
                pe.wait_ge(slots_out, NG * (t + 1))
                pe.wait_ge(extra_out, 2 * (t + 1))
                if t == 0:
                    pe.wait_ge(look_out, LOOKED_UP)
                if t >= 2:
                    pe.wait_ge(prods_dve, BY_ENGINE * (t - 1))
                    pe.wait_ge(prods_act, BY_ENGINE * (t - 1))
                for blk in range(BLOCKS):
                    for q in range(QUADS):
                        x = vecs_t[:, t, QUADS * blk + q, :]
                        mm = nc.tensor.matmul(gram[t % 2][QUAD * q:QUAD * q + ROWS, blk, 0:N], x[:, 0:ROWS],
                                              x[:, 0:N], start=True, stop=True)
                mm.then_inc(gram_ok, 1)

            pe.wait_ge(ident_ok, 1)
            pe.wait_ge(dense_in, 16)
            k = 0
            for step, t, i in TENSOR_STEPS:
                if step == "turn":
                    turn(k, t, i)
                    k += 1
                elif step == "look":
                    look_up(k, t)
                    k += 1
                elif step == "products":
                    products(t)
                elif step == "layer1":
                    mlp1(t, i)
                elif step == "layer2":
                    mlp2(t)
                else:
                    mlp3(t)

        @block.vector
        def _(dve):
            def copy_y(t):
                dve.wait_ge(y_ok, t + 1)
                nc.vector.tensor_copy(y_sb[:, t * P:(t + 1) * P], h2_ps[0:1, 3, :]).then_inc(y_out, 1)

            nc.vector.memset(one[:], 1.0).then_inc(one_ok, 1)
            nc.vector.memset(prods[:], 0.0).then_inc(prods_zero, 1)

            def make_one_hot(j):
                if j == 0:
                    dve.wait_ge(rows_ok, 2 * len(SIZES))
                dve.wait_ge(ids_all_in[j], 16)
                if j >= 2:
                    dve.wait_ge(look_ok, j - 1)
                for c in range(FULL[j] + 1 - BY_SCALAR):
                    at = row_of[:, SIZES.index(FULL[j]), c:c + 1]
                    nc.vector.tensor_scalar(one_hot[:, j % 2, c, :], ids_all[:, j, :], at, None,
                                            ALU.is_equal).then_inc(hot_ok, 1)

            def split_table(j):
                dve.wait_ge(hi_ok, j + 1)
                nb = FULL[j] + 1
                nc.vector.tensor_tensor(table_lo[:, j % 2, 0:nb, :], table[:, j % 2, 0:nb, :],
                                        table_hi[:, j % 2, 0:nb, :].bitcast(F32), ALU.subtract).then_inc(lo_ok, 1)

            def copy_slots(t, g):
                k = UNITS.index(("turn", t, g))
                dve.wait_ge(turned_ok, NG * t + g + 1)
                slots = GROUPS[g]
                nc.vector.tensor_copy(
                    vecs_t[:, t, :, slots[0]:slots[-1] + 1].rearrange("d r s -> d s r"),
                    turned[k % 2][:, 0:len(slots), :]).then_inc(slots_out, 1)

            split_table(0)
            make_one_hot(0)
            for n in range(len(FIRST_TURNS)):
                if n + 1 < LOOKED_UP:
                    split_table(n + 1)
                    make_one_hot(n + 1)
                copy_slots(*FIRST_TURNS[n][1:])
            dve.wait_ge(w_in, 48)
            nc.vector.tensor_tensor(w_dense[:], w1_sb[:, 0, :], w1_sb[:, 1, :], ALU.add)\
                .then_inc(w_dense_ok, 1)
            dve.wait_ge(prods_zero, 1)
            for step, t in VECTOR_STEPS:
                if step == "turn":
                    for g in range(NG):
                        copy_slots(t, g)
                elif step == "products":
                    copy_products(dve, nc.vector.tensor_copy, prods_dve, t, [0, 1])
                else:
                    copy_y(t)

        @block.scalar
        def _(act):
            def relu1(t):
                if t == 0:
                    act.wait_ge(w_in, 48)
                if t >= 2:
                    act.wait_ge(h2_ok, t - 1)
                for o in range(H1 // P):
                    act.wait_ge(h1_ok, t + 1)
                    nc.scalar.activation(h1[:, t % 2, o, :], h1_ps[:, o, :], ACT.Relu,
                                         bias=b1_col[:, o:o + 1]).then_inc(h1_out, 1)

            def relu2(t):
                if t >= 2:
                    act.wait_ge(y_ok, t - 1)
                for o in range(H2 // P):
                    act.wait_ge(h2_ok, t + 1)
                    nc.scalar.activation(h2[:, t % 2, o, :], h2_ps[:, o, :], ACT.Relu,
                                         bias=b2_col[:, o:o + 1]).then_inc(h2_out, 1)

            def table_hi_part(j):
                nb = FULL[j] + 1
                act.wait_ge(table_in[j % 2], 32 * (j // 2 + 1))
                if j >= 2:
                    act.wait_ge(look_ok, j - 1)
                nc.scalar.copy(table_hi[:, j % 2, 0:nb, :], table[:, j % 2, 0:nb, :]).then_inc(hi_ok, 1)

            def make_one_hot_blocks(j):
                if j == 0:
                    act.wait_ge(rows_ok, 2 * len(SIZES))
                    act.wait_ge(one_ok, 1)
                act.wait_ge(ids_all_in[j], 16)
                blocks = range(FULL[j] + 1 - BY_SCALAR, FULL[j] + 1)
                for i, c in enumerate(blocks):
                    if j >= 1:
                        act.wait_ge(hot_scalar, BY_SCALAR * (j - 1) + i + 1)
                    at = row_of[:, SIZES.index(FULL[j]), c:c + 1]
                    nc.scalar.activation(distance[:, i, :], ids_all[:, j, :], ACT.Square, bias=at,
                                         scale=-1.0).then_inc(distance_ok, 1)
                if j >= 2:
                    act.wait_ge(look_ok, j - 1)
                for i, c in enumerate(blocks):
                    act.wait_ge(distance_ok, BY_SCALAR * j + i + 1)
                    nc.scalar.activation(one_hot[:, j % 2, c, :], distance[:, i, :], ACT.Relu, bias=one[:],
                                         scale=-1.0).then_inc(hot_scalar, 1)

            def slots_of_lookup(j):
                k = UNITS.index(("look", j, 0))
                act.wait_ge(look_ok, j + 1)
                nc.scalar.copy(vecs_t[:, :, :, TURNED + j], turned[k % 2][:]).then_inc(look_out, 1)

            def extra_copies(t):
                act.wait_ge(slots_out, NG * t + 1)
                nc.scalar.copy(dense_t[:, t, :], vecs_t[:, t, :, 0]).then_inc(extra_out, 1)
                nc.scalar.copy(vecs_t[:, t, :, N:ROWS], vecs_t[:, t, :, 0:REPEAT]).then_inc(extra_out, 1)

            for j in range(2):
                table_hi_part(j)
                make_one_hot_blocks(j)
            extra_copies(0)
            for j in range(LOOKED_UP):
                slots_of_lookup(j)
                if j + 2 < LOOKED_UP:
                    table_hi_part(j + 2)
                    make_one_hot_blocks(j + 2)
            act.wait_ge(prods_zero, 1)
            for step, t in SCALAR_STEPS:
                if step == "extra":
                    extra_copies(t)
                elif step == "products":
                    copy_products(act, nc.scalar.copy, prods_act, t, [2, 3])
                elif step == "layer1":
                    relu1(t)
                else:
                    relu2(t)


def kernel(**inputs):
    import numpy as np
    import concourse.bacc as bacc
    from concourse.bass_utils import run_bass_kernel_spmd

    nc = bacc.Bacc("TRN2", target_bir_lowering=False, num_devices=1)
    arrays = {}

    def given(name, a):
        a = np.ascontiguousarray(a)
        arrays[name] = a
        return nc.dram_tensor(name, a.shape, mybir.dt.from_np(a.dtype), kind="ExternalInput").ap()

    w = np.asarray(inputs["W_top1"])
    w1 = np.zeros((P, 2 + CHUNKS, H1), w.dtype)
    w1[:, 0] = w[0:D]
    w1[:, 1] = w[w.shape[0] - D:]
    number = {}
    for n in range(N):
        for m in range(n + 1, N):
            number[n, m] = len(number)
    feature = [0] + [1 + f for f in SLOT_TABLE[1:]]
    for (c, p), pair in product_rows().items():
        w1[p, 2 + c] = w[D + number[tuple(sorted(feature[s] for s in pair))]]
    w2 = np.asarray(inputs["W_top2"]).reshape(H1 // P, P, H2).transpose(1, 0, 2)
    cols = [np.asarray(inputs[k]).reshape(-1, P).T for k in ("b_top1", "b_top2", "W_top3")]

    dense = given("dense", inputs["r_dense_features"])
    ids = given("ids", inputs["ids"])
    ids_t = given("ids_t", np.asarray(inputs["ids"]).T)
    tables = [given(f"tbl_{f}", inputs[f"tbl_{f}"]) for f in range(F)]
    w1 = given("w1", w1)
    w2 = given("w2", w2)
    small = given("small", np.concatenate(cols, axis=1))
    out = nc.dram_tensor("y", (B, 1), F32, kind="ExternalOutput").ap()
    dlrm_tower(nc, dense, ids, ids_t, tables, w1, w2, small, out)
    r = run_bass_kernel_spmd(nc, [arrays], core_ids=[0])
    return r.results[0]["y"]
```

```python
from contextlib import ExitStack

import concourse.bass as bass
from concourse import mybir

F32 = mybir.dt.float32
I32 = mybir.dt.int32
U32 = mybir.dt.uint32
F32R = mybir.dt.float32r
ALU = mybir.AluOpType
ACT = mybir.ActivationFunctionType

P = 128
B = 512
D = 128
F = 26
N = F + 1
TILES = B // P
H1, H2 = 512, 256
QUAD = 32
QUADS = P // QUAD
BLOCKS = P // QUADS
CHUNKS = 6
REPEAT = 2
ROWS = N + REPEAT
TABLE_ROWS = [125000, 1000, 12500, 12500, 12500, 1250, 1000, 12500, 12500, 1250, 12500, 12500, 1250,
              12500, 1000, 1250, 1250, 1250, 1000, 1000, 1000, 1000, 1000, 1250, 1250, 1250]
LOOKED_UP = 7
by_size = sorted(range(F), key=lambda f: TABLE_ROWS[f])
LOOKUPS = by_size[:LOOKED_UP]
GATHERED = by_size[LOOKED_UP:]
SLOT_TABLE = [None] + GATHERED + LOOKUPS
TURNED = 1 + len(GATHERED)
FULL = [TABLE_ROWS[f] // P for f in LOOKUPS]
LAST = [TABLE_ROWS[f] % P for f in LOOKUPS]
MAX_BLOCKS = max(FULL) + 1
PARTS = 3
BY_SCALAR = 2
SIZES = sorted(set(FULL))
PER_GROUP = 4
GROUPS = [list(range(a, min(a + PER_GROUP, TURNED))) for a in range(0, TURNED, PER_GROUP)]
NG = len(GROUPS)
QUARTERS = H1 // P


def turns(t, first, end):
    return [("turn", t, g) for g in range(first, end)]


def first_layer(t):
    return [("layer1", t, q) for q in range(QUARTERS)]


EARLY = 2
FIRST_TURNS = turns(0, 0, NG) + turns(1, 0, EARLY)
FIRST_LOOKS = [("look", j, 0) for j in range(LOOKED_UP)]
FIRST_STEPS = [x for pair in zip(FIRST_TURNS[:NG], FIRST_LOOKS) for x in pair]
FIRST_STEPS += FIRST_LOOKS[NG:] + FIRST_TURNS[NG:]
TENSOR_STEPS = (
    FIRST_STEPS + [("products", 0, 0)] + turns(1, EARLY, EARLY + 2) + first_layer(0)[:1]
    + turns(1, EARLY + 2, NG) + first_layer(0)[1:]
    + [("products", 1, 0)] + turns(2, 0, 2) + [("layer2", 0, 0)] + first_layer(1)[:2]
    + turns(2, 2, 3) + first_layer(1)[2:3] + turns(2, 3, 4) + first_layer(1)[3:] + turns(2, 4, NG)
    + [("layer3", 0, 0), ("products", 2, 0)]
    + turns(3, 0, 2) + [("layer2", 1, 0)] + first_layer(2)[:1] + turns(3, 2, 3) + first_layer(2)[1:2]
    + turns(3, 3, 4) + first_layer(2)[2:] + turns(3, 4, NG)
    + [("layer3", 1, 0), ("products", 3, 0), ("layer2", 2, 0)]
    + first_layer(3) + [("layer3", 2, 0), ("layer2", 3, 0), ("layer3", 3, 0)]
)
VECTOR_STEPS = [
    ("products", 0), ("turn", 1), ("products", 1), ("turn", 2), ("layer3", 0), ("products", 2),
    ("turn", 3), ("layer3", 1), ("products", 3), ("layer3", 2), ("layer3", 3),
]
SCALAR_STEPS = [
    ("extra", 1), ("products", 0), ("layer1", 0), ("products", 1), ("extra", 2), ("layer2", 0),
    ("layer1", 1), ("products", 2), ("extra", 3), ("layer2", 1), ("layer1", 2),
    ("products", 3), ("layer2", 2), ("layer1", 3), ("layer2", 3),
]
FIRST_SLOT = [6, 12, 18, 0]
LATE_SLOT = 24


def product_rows():
    where = {}
    for q in range(QUADS):
        for c in range(CHUNKS):
            late = q == QUADS - 1 and c < N - LATE_SLOT
            m = LATE_SLOT + c if late else FIRST_SLOT[q] + c
            for n in range(m):
                where[c, QUAD * q + n] = (n, m)
            if late:
                for n in range(c):
                    where[c, QUAD * q + N + n] = (n, c)
    assert sorted(where.values()) == [(n, m) for n in range(N) for m in range(n + 1, N)]
    return where


def dlrm_tower(nc, dense, ids, ids_t, tables, w1, w2, small, out):
    with ExitStack() as ctx:
        def sb(name, shape, dt=F32):
            return ctx.enter_context(nc.sbuf_tensor(name, shape, dt))

        def psum(name, shape):
            return ctx.enter_context(nc.psum_tensor(name, shape, F32))

        def sem(name):
            return ctx.enter_context(nc.semaphore(name))

        idx = sb("idx", [P, TILES, F], I32)
        dense_rows = sb("dense_rows", [P, TILES, D])
        vecs = sb("vecs", [P, 2, TURNED, D])
        vecs_t = sb("vecs_t", [P, TILES, P, ROWS])
        dense_t = sb("dense_t", [P, TILES, P])
        ident = sb("ident", [P, P])
        w1_sb = sb("w1_sb", [P, 2 + CHUNKS, H1])
        w_dense = sb("w_dense", [P, H1])
        w2_sb = sb("w2_sb", [P, H1 // P, H2])
        small_sb = sb("small_sb", [P, 8])
        b1_col, b2_col, w3_col = small_sb[:, 0:4], small_sb[:, 4:6], small_sb[:, 6:8]
        prods = sb("prods", [P, 2, CHUNKS, P])
        h1 = sb("h1", [P, 2, H1 // P, P])
        h2 = sb("h2", [P, 2, H2 // P, P])
        y_sb = sb("y_sb", [1, B])
        ids_all = sb("ids_all", [P, LOOKED_UP, B], I32)
        row_of = sb("row_of", [P, len(SIZES), MAX_BLOCKS])
        table = sb("table", [P, 2, MAX_BLOCKS, D])
        table_hi = sb("table_hi", [P, PARTS, MAX_BLOCKS, D], F32R)
        table_lo = sb("table_lo", [P, PARTS, MAX_BLOCKS, D], F32R)
        one_hot = sb("one_hot", [P, 2, MAX_BLOCKS, B], F32R)

        turned = [psum(f"turned{i}", [P, PER_GROUP, P]) for i in range(2)]
        gram = [psum(f"gram{i}", [P, BLOCKS, QUAD]) for i in range(2)]
        looked_up = [g[:, 0:BLOCKS // 2, :].rearrange("p b s -> p (b s)") for g in gram]
        h1_ps = psum("h1_ps", [P, H1 // P, P])
        h2_ps = psum("h2_ps", [P, H1 // P, P])

        idx_in = sem("idx_in")
        dense_in = sem("dense_in")
        w_in = sem("w_in")
        distance = sb("distance", [P, BY_SCALAR, B])
        one = sb("one", [P, 1])
        one_ok = sem("one_ok")
        distance_ok = sem("distance_ok")
        hot_scalar = sem("hot_scalar")
        ids_all_in = [sem(f"ids_all_in{j}") for j in range(LOOKED_UP)]
        table_in = [sem(f"table_in{i}") for i in range(2)]
        table_zero = sem("table_zero")
        rows_ok = sem("rows_ok")
        hi_ok = sem("hi_ok")
        lo_ok = sem("lo_ok")
        hot_ok = sem("hot_ok")
        look_ok = sem("look_ok")
        look_out = sem("look_out")
        gathered = [[sem(f"gathered{t}_{g}") for g in range(len(GROUPS))] for t in range(TILES)]
        ident_zero = sem("ident_zero")
        ident_ok = sem("ident_ok")
        prods_zero = sem("prods_zero")
        w_dense_ok = sem("w_dense_ok")
        turned_ok = sem("turned_ok")
        slots_out = sem("slots_out")
        extra_out = sem("extra_out")
        gram_ok = sem("gram_ok")
        prods_dve = sem("prods_dve")
        prods_act = sem("prods_act")
        h1_ok = sem("h1_ok")
        h1_out = sem("h1_out")
        h2_ok = sem("h2_ok")
        h2_out = sem("h2_out")
        y_ok = sem("y_ok")
        y_out = sem("y_out")
        stored = sem("stored")

        BY_ENGINE = 2 * (QUADS + 1)

        def copy_products(engine, copy, done, t, quads):
            engine.wait_ge(gram_ok, t + 1)
            if t >= 2:
                engine.wait_ge(h1_ok, t - 1)
            for i, q in enumerate(quads):
                src = gram[t % 2][QUAD * q:QUAD * (q + 1), :, :]
                for k in [3, 0, 1, 2]:
                    copy(prods[QUAD * k:QUAD * k + ROWS, t % 2, :, q::QUADS],
                         src[0:ROWS, :, FIRST_SLOT[k]:FIRST_SLOT[k] + CHUNKS]
                         .rearrange("p b c -> p c b")).then_inc(done, 1)
                engine.wait_ge(done, BY_ENGINE * t + (QUADS + 1) * i + 1)
                copy(prods[QUAD * 3:QUAD * 3 + N, t % 2, 0:N - LATE_SLOT, q::QUADS],
                     src[0:N, :, LATE_SLOT:N].rearrange("p b c -> p c b")).then_inc(done, 1)

        block = ctx.enter_context(nc.Block())

        @block.sync
        def _(sp):
            sp.dma_start(idx[:], ids.rearrange("(t p) f -> p t f", p=P)).then_inc(idx_in, 16)

            def load_table(j):
                f, full, last = LOOKUPS[j], FULL[j], LAST[j]
                if j == 0:
                    sp.wait_ge(table_zero, len(SIZES))
                if j >= 2:
                    sp.wait_ge(lo_ok, j - 1)
                sp.dma_start(table[:, j % 2, 0:full, :],
                             tables[f][0:full * P, :].rearrange("(p c) d -> p c d", p=P))\
                    .then_inc(table_in[j % 2], 16)
                sp.dma_start(table[0:last, j % 2, full, :], tables[f][full * P:full * P + last, :])\
                    .then_inc(table_in[j % 2], 16)
                sp.dma_start(ids_all[:, j, :], ids_t[f:f + 1, :].to_broadcast([P, B]))\
                    .then_inc(ids_all_in[j], 16)

            load_table(0)
            sp.dma_start(dense_rows[:], dense.rearrange("(t p) d -> p t d", p=P)).then_inc(dense_in, 16)
            for j in range(1, LOOKED_UP):
                load_table(j)
            sp.dma_start(w1_sb[:], w1).then_inc(w_in, 16)
            sp.dma_start(w2_sb[:], w2).then_inc(w_in, 16)
            sp.dma_start(small_sb[:], small).then_inc(w_in, 16)
            sp.wait_ge(y_out, TILES)
            sp.dma_start(out.rearrange("b o -> o b"), y_sb[:]).then_inc(stored, 16)
            sp.wait_ge(stored, 16)

        @block.gpsimd
        def _(pool):
            nc.gpsimd.memset(ident[:], 0.0).then_inc(ident_zero, 1)
            pool.wait_ge(ident_zero, 1)
            nc.gpsimd.affine_select(out=ident[:], in_=ident[:], compare_op=ALU.not_equal, fill=1.0, base=0,
                                    pattern=[[-1, P]], channel_multiplier=1).then_inc(ident_ok, 1)
            for i, full in enumerate(SIZES):
                nc.gpsimd.iota(row_of[:, i, 0:full], pattern=[[1, full]], base=0, channel_multiplier=full,
                               allow_small_or_imprecise_dtypes=True).then_inc(rows_ok, 1)
                nc.gpsimd.iota(row_of[:, i, full:full + 1], pattern=[[1, 1]], base=full * P,
                               channel_multiplier=1,
                               allow_small_or_imprecise_dtypes=True).then_inc(rows_ok, 1)
            pool.wait_ge(idx_in, 16)
            for t in range(TILES):
                for g, slots in enumerate(GROUPS):
                    if t >= 2:
                        pool.wait_ge(turned_ok, NG * (t - 2) + g + 1)
                    for s in slots:
                        if s:
                            f = SLOT_TABLE[s]
                            nc.gpsimd.indirect_dma_start(
                                out=vecs[:, t % 2, s, :], out_offset=None, in_=tables[f],
                                in_offset=bass.IndirectOffsetOnAxis(
                                    ap=idx[:, t, f:f + 1].bitcast(U32), axis=0),
                            ).then_inc(gathered[t][g], 16)

        @block.tensor
        def _(pe):
            def mlp1(t, o):
                if o == 0:
                    first_layer_ready(t)
                cols = slice(o * P, (o + 1) * P)
                nc.tensor.matmul(h1_ps[:, o, :], w_dense[:, cols], dense_t[:, t, :], start=True, stop=False)
                for c in range(CHUNKS):
                    mm = nc.tensor.matmul(h1_ps[:, o, :], w1_sb[:, 2 + c, cols], prods[:, t % 2, c, :],
                                          start=False, stop=(c == CHUNKS - 1))
                if o == QUARTERS - 1:
                    mm.then_inc(h1_ok, 1)

            def first_layer_ready(t):
                pe.wait_ge(prods_dve, BY_ENGINE * (t + 1))
                pe.wait_ge(prods_act, BY_ENGINE * (t + 1))
                if t == 0:
                    pe.wait_ge(w_in, 48)
                    pe.wait_ge(w_dense_ok, 1)
                if t >= 1:
                    pe.wait_ge(h1_out, 4 * t)

            def mlp2(t):
                pe.wait_ge(h1_out, 4 * (t + 1))
                if t >= 1:
                    pe.wait_ge(y_out, t)
                for o in range(H2 // P):
                    for c in range(H1 // P):
                        mm = nc.tensor.matmul(h2_ps[:, o, :], w2_sb[:, c, o * P:(o + 1) * P], h1[:, t % 2, c, :],
                                              start=(c == 0), stop=(c == H1 // P - 1))
                mm.then_inc(h2_ok, 1)

            def mlp3(t):
                pe.wait_ge(h2_out, 2 * (t + 1))
                for c in range(H2 // P):
                    mm = nc.tensor.matmul(h2_ps[0:1, 3, :], w3_col[:, c:c + 1], h2[:, t % 2, c, :],
                                          start=(c == 0), stop=(c == H2 // P - 1))
                mm.then_inc(y_ok, 1)

            def turn(t, g):
                slots = GROUPS[g]
                pe.wait_ge(gathered[t][g], 16 * sum(s > 0 for s in slots))
                k = NG * t + g
                if k >= 2:
                    pe.wait_ge(slots_out, k - 1)
                for j, s in enumerate(slots):
                    mm = nc.tensor.transpose(turned[k % 2][:, j, :],
                                             vecs[:, t % 2, s, :] if s else dense_rows[:, t, :], ident[:])
                mm.then_inc(turned_ok, 1)

            def look_up(j):
                if j >= 2:
                    pe.wait_ge(look_out, j - 1)
                pe.wait_ge(lo_ok, j + 1)
                for c in range(FULL[j] + 1):
                    rows = P if c < FULL[j] else LAST[j]
                    by_vector = FULL[j] + 1 - BY_SCALAR
                    if c < by_vector:
                        pe.wait_ge(hot_ok, sum(n + 1 - BY_SCALAR for n in FULL[:j]) + c + 1)
                    else:
                        pe.wait_ge(hot_scalar, BY_SCALAR * j + c - by_vector + 1)
                    for part in (table_hi, table_lo):
                        mm = nc.tensor.matmul(looked_up[j % 2],
                                              part[0:rows, j % PARTS, c, :], one_hot[0:rows, j % 2, c, :],
                                              start=(c == 0 and part is table_hi),
                                              stop=(c == FULL[j] and part is table_lo))
                mm.then_inc(look_ok, 1)

            def products(t):
                pe.wait_ge(slots_out, NG * (t + 1))
                pe.wait_ge(extra_out, 2 * (t + 1))
                if t == 0:
                    pe.wait_ge(look_out, LOOKED_UP)
                if t >= 2:
                    pe.wait_ge(prods_dve, BY_ENGINE * (t - 1))
                    pe.wait_ge(prods_act, BY_ENGINE * (t - 1))
                for blk in range(BLOCKS):
                    for q in range(QUADS):
                        x = vecs_t[:, t, QUADS * blk + q, :]
                        mm = nc.tensor.matmul(gram[t % 2][QUAD * q:QUAD * q + ROWS, blk, 0:N], x[:, 0:ROWS],
                                              x[:, 0:N], start=True, stop=True)
                mm.then_inc(gram_ok, 1)

            pe.wait_ge(ident_ok, 1)
            pe.wait_ge(dense_in, 16)
            for step, t, i in TENSOR_STEPS:
                if step == "turn":
                    turn(t, i)
                elif step == "look":
                    look_up(t)
                elif step == "products":
                    products(t)
                elif step == "layer1":
                    mlp1(t, i)
                elif step == "layer2":
                    mlp2(t)
                else:
                    mlp3(t)

        @block.vector
        def _(dve):
            def copy_y(t):
                dve.wait_ge(y_ok, t + 1)
                nc.vector.tensor_copy(y_sb[:, t * P:(t + 1) * P], h2_ps[0:1, 3, :]).then_inc(y_out, 1)

            for full in SIZES:
                nc.vector.memset(table[:, :, full, :], 0.0).then_inc(table_zero, 1)
            nc.vector.memset(one[:], 1.0).then_inc(one_ok, 1)
            nc.vector.memset(prods[:], 0.0).then_inc(prods_zero, 1)

            def make_one_hot(j):
                if j == 0:
                    dve.wait_ge(rows_ok, 2 * len(SIZES))
                dve.wait_ge(ids_all_in[j], 16)
                if j >= 2:
                    dve.wait_ge(look_ok, j - 1)
                for c in range(FULL[j] + 1 - BY_SCALAR):
                    at = row_of[:, SIZES.index(FULL[j]), c:c + 1]
                    nc.vector.tensor_scalar(one_hot[:, j % 2, c, :], ids_all[:, j, :], at, None,
                                            ALU.is_equal).then_inc(hot_ok, 1)

            def split_table(j):
                dve.wait_ge(hi_ok, j + 1)
                nb = FULL[j] + 1
                nc.vector.tensor_tensor(table_lo[:, j % PARTS, 0:nb, :], table[:, j % 2, 0:nb, :],
                                        table_hi[:, j % PARTS, 0:nb, :].bitcast(F32), ALU.subtract).then_inc(lo_ok, 1)

            def copy_slots(t, g):
                k = NG * t + g
                dve.wait_ge(turned_ok, k + 1)
                slots = GROUPS[g]
                nc.vector.tensor_copy(
                    vecs_t[:, t, :, slots[0]:slots[-1] + 1].rearrange("d r s -> d s r"),
                    turned[k % 2][:, 0:len(slots), :]).then_inc(slots_out, 1)

            split_table(0)
            make_one_hot(0)
            for n in range(NG):
                split_table(n + 1)
                make_one_hot(n + 1)
                copy_slots(*FIRST_TURNS[n][1:])
            for j in range(NG + 1, LOOKED_UP):
                split_table(j)
                make_one_hot(j)
            for step in FIRST_TURNS[NG:]:
                copy_slots(*step[1:])
            dve.wait_ge(w_in, 48)
            nc.vector.tensor_tensor(w_dense[:], w1_sb[:, 0, :], w1_sb[:, 1, :], ALU.add)\
                .then_inc(w_dense_ok, 1)
            dve.wait_ge(prods_zero, 1)
            for step, t in VECTOR_STEPS:
                if step == "turn":
                    for g in range(EARLY if t == 1 else 0, NG):
                        copy_slots(t, g)
                elif step == "products":
                    copy_products(dve, nc.vector.tensor_copy, prods_dve, t, [0, 1])
                else:
                    copy_y(t)

        @block.scalar
        def _(act):
            def relu1(t):
                if t == 0:
                    act.wait_ge(w_in, 48)
                if t >= 2:
                    act.wait_ge(h2_ok, t - 1)
                for o in range(H1 // P):
                    act.wait_ge(h1_ok, t + 1)
                    nc.scalar.activation(h1[:, t % 2, o, :], h1_ps[:, o, :], ACT.Relu,
                                         bias=b1_col[:, o:o + 1]).then_inc(h1_out, 1)

            def relu2(t):
                if t >= 2:
                    act.wait_ge(y_ok, t - 1)
                for o in range(H2 // P):
                    act.wait_ge(h2_ok, t + 1)
                    nc.scalar.activation(h2[:, t % 2, o, :], h2_ps[:, o, :], ACT.Relu,
                                         bias=b2_col[:, o:o + 1]).then_inc(h2_out, 1)

            def table_hi_part(j):
                nb = FULL[j] + 1
                act.wait_ge(table_in[j % 2], 32 * (j // 2 + 1))
                if j >= PARTS:
                    act.wait_ge(look_ok, j - PARTS + 1)
                nc.scalar.copy(table_hi[:, j % PARTS, 0:nb, :], table[:, j % 2, 0:nb, :]).then_inc(hi_ok, 1)

            def make_one_hot_blocks(j):
                if j == 0:
                    act.wait_ge(rows_ok, 2 * len(SIZES))
                    act.wait_ge(one_ok, 1)
                act.wait_ge(ids_all_in[j], 16)
                blocks = range(FULL[j] + 1 - BY_SCALAR, FULL[j] + 1)
                for i, c in enumerate(blocks):
                    if j >= 1:
                        act.wait_ge(hot_scalar, BY_SCALAR * (j - 1) + i + 1)
                    at = row_of[:, SIZES.index(FULL[j]), c:c + 1]
                    nc.scalar.activation(distance[:, i, :], ids_all[:, j, :], ACT.Square, bias=at,
                                         scale=-1.0).then_inc(distance_ok, 1)
                if j >= 2:
                    act.wait_ge(look_ok, j - 1)
                for i, c in enumerate(blocks):
                    act.wait_ge(distance_ok, BY_SCALAR * j + i + 1)
                    nc.scalar.activation(one_hot[:, j % 2, c, :], distance[:, i, :], ACT.Relu, bias=one[:],
                                         scale=-1.0).then_inc(hot_scalar, 1)

            def slots_of_lookup(j):
                act.wait_ge(look_ok, j + 1)
                nc.scalar.copy(vecs_t[:, :, :, TURNED + j],
                               looked_up[j % 2].rearrange("p (t r) -> p t r", t=TILES)).then_inc(look_out, 1)

            def extra_copies(t):
                act.wait_ge(slots_out, NG * t + 1)
                nc.scalar.copy(dense_t[:, t, :], vecs_t[:, t, :, 0]).then_inc(extra_out, 1)
                nc.scalar.copy(vecs_t[:, t, :, N:ROWS], vecs_t[:, t, :, 0:REPEAT]).then_inc(extra_out, 1)

            for j in range(2):
                table_hi_part(j)
                make_one_hot_blocks(j)
            table_hi_part(2)
            extra_copies(0)
            for j in range(LOOKED_UP):
                slots_of_lookup(j)
                if j + 2 < LOOKED_UP:
                    make_one_hot_blocks(j + 2)
                if j + 3 < LOOKED_UP:
                    table_hi_part(j + 3)
            act.wait_ge(prods_zero, 1)
            for step, t in SCALAR_STEPS:
                if step == "extra":
                    extra_copies(t)
                elif step == "products":
                    copy_products(act, nc.scalar.copy, prods_act, t, [2, 3])
                elif step == "layer1":
                    relu1(t)
                else:
                    relu2(t)


def kernel(**inputs):
    import numpy as np
    import concourse.bacc as bacc
    from concourse.bass_utils import run_bass_kernel_spmd

    nc = bacc.Bacc("TRN2", target_bir_lowering=False, num_devices=1)
    arrays = {}

    def given(name, a):
        a = np.ascontiguousarray(a)
        arrays[name] = a
        return nc.dram_tensor(name, a.shape, mybir.dt.from_np(a.dtype), kind="ExternalInput").ap()

    w = np.asarray(inputs["W_top1"])
    w1 = np.zeros((P, 2 + CHUNKS, H1), w.dtype)
    w1[:, 0] = w[0:D]
    w1[:, 1] = w[w.shape[0] - D:]
    number = {}
    for n in range(N):
        for m in range(n + 1, N):
            number[n, m] = len(number)
    feature = [0] + [1 + f for f in SLOT_TABLE[1:]]
    for (c, p), pair in product_rows().items():
        w1[p, 2 + c] = w[D + number[tuple(sorted(feature[s] for s in pair))]]
    w2 = np.asarray(inputs["W_top2"]).reshape(H1 // P, P, H2).transpose(1, 0, 2)
    cols = [np.asarray(inputs[k]).reshape(-1, P).T for k in ("b_top1", "b_top2", "W_top3")]

    dense = given("dense", inputs["r_dense_features"])
    ids = given("ids", inputs["ids"])
    ids_t = given("ids_t", np.asarray(inputs["ids"]).T)
    tables = [given(f"tbl_{f}", inputs[f"tbl_{f}"]) for f in range(F)]
    w1 = given("w1", w1)
    w2 = given("w2", w2)
    small = given("small", np.concatenate(cols, axis=1))
    out = nc.dram_tensor("y", (B, 1), F32, kind="ExternalOutput").ap()
    dlrm_tower(nc, dense, ids, ids_t, tables, w1, w2, small, out)
    r = run_bass_kernel_spmd(nc, [arrays], core_ids=[0])
    return r.results[0]["y"]
```
